# Optimizing a Trainium2 kernel written in Bass

```python
import numpy as np
import jax
import jax.numpy as jnp

def _softmax(x, axis=-1):
    return jax.nn.softmax(x, axis=axis)
def _gelu(x):
    return jax.nn.gelu(x, approximate=True)
def _silu(x):
    return jax.nn.silu(x)
def _sigmoid(x):
    return jax.nn.sigmoid(x)
def _layernorm(x, axis=-1, eps=1e-5):
    m = jnp.mean(x, axis=axis, keepdims=True)
    v = jnp.var(x, axis=axis, keepdims=True)
    return (x - m) / jnp.sqrt(v + eps)
def _scatter_add(tgt, idx, src, axis=0):
    return tgt.at[idx].add(src)
def _segment_sum(src, seg, n):
    return jax.ops.segment_sum(src, seg, n)

kernel_name = 'mk_conv_preact_d2_conv_nchw512_9b6a3e'

def setup_inputs(seed: int = 0):
    np.random.seed(seed)
    _w = jnp.asarray
    def _rec_inputs():
        import jax
        import jax.numpy as jnp
        _gk = jax.random.key(seed)
        x = -0.000125 + 0.9999 * jax.random.normal(jax.random.fold_in(_gk, 1), (16, 512, 64, 64), jnp.float32)
        return x
    x = _rec_inputs()
    def _L0_conv_setup():
        import jax, jax.numpy as jnp
        import numpy as np
        THRESHOLD = 0.625
        key = jax.random.key(seed)
        k1, k2 = jax.random.split(key)
        x = jax.random.normal(k1, (16, 512, 64, 64), dtype=jnp.float32)
        negative_dict = 0.02 * jax.random.truncated_normal(k2, -2.0, 2.0, (512, 512), dtype=jnp.float32)
        return {'x': x, 'negative_dict': negative_dict}
    _L0_conv_all = _L0_conv_setup()
    _L0_conv_in = {k: v for k, v in _L0_conv_all.items() if k in ('negative_dict', )}
    del _L0_conv_all

    def _L1_conv_setup():
        import jax, jax.numpy as jnp
        import numpy as np
        from jax import lax
        B, C, H, W = (32, 512, 56, 56)
        CO = 512
        EPS = 1e-05

        def binarize(x):
            xc = jnp.clip(x, -1.0, 1.0)
            return xc + lax.stop_gradient(jnp.sign(x) - xc)

        def batchnorm(y, g, b, m, v):
            inv = g * lax.rsqrt(v + EPS)
            return y * inv[None, :, None, None] + (b - m * inv)[None, :, None, None]
        key = jax.random.key(seed)
        ks = jax.random.split(key, 11)
        return {'x': jax.random.normal(ks[0], (B, C, H, W), dtype=jnp.float32), 'w_dw': jax.random.normal(ks[1], (C, 1, 3, 3), dtype=jnp.float32), 'w_pw': jax.random.normal(ks[2], (CO, C, 1, 1), dtype=jnp.float32), 'g1': jax.random.uniform(ks[3], (C,), dtype=jnp.float32), 'b1': jax.random.normal(ks[4], (C,), dtype=jnp.float32), 'm1': jax.random.normal(ks[5], (C,), dtype=jnp.float32), 'v1': jax.random.uniform(ks[6], (C,), dtype=jnp.float32), 'g2': jax.random.uniform(ks[7], (CO,), dtype=jnp.float32), 'b2': jax.random.normal(ks[8], (CO,), dtype=jnp.float32), 'm2': jax.random.normal(ks[9], (CO,), dtype=jnp.float32), 'v2': jax.random.uniform(ks[10], (CO,), dtype=jnp.float32)}
    _L1_conv_all = _L1_conv_setup()
    _L1_conv_in = {k: v for k, v in _L1_conv_all.items() if k in ('w_dw', 'w_pw', 'g1', 'b1', 'm1', 'v1', 'g2', 'b2', 'm2', 'v2', )}
    del _L1_conv_all

    return {
        "x": x,
        "L0_conv_negative_dict": _L0_conv_in["negative_dict"],
        "L1_conv_w_dw": _L1_conv_in["w_dw"],
        "L1_conv_w_pw": _L1_conv_in["w_pw"],
        "L1_conv_g1": _L1_conv_in["g1"],
        "L1_conv_b1": _L1_conv_in["b1"],
        "L1_conv_m1": _L1_conv_in["m1"],
        "L1_conv_v1": _L1_conv_in["v1"],
        "L1_conv_g2": _L1_conv_in["g2"],
        "L1_conv_b2": _L1_conv_in["b2"],
        "L1_conv_m2": _L1_conv_in["m2"],
        "L1_conv_v2": _L1_conv_in["v2"],
    }

def reference(x, L0_conv_negative_dict, L1_conv_w_dw, L1_conv_w_pw, L1_conv_g1, L1_conv_b1, L1_conv_m1, L1_conv_v1, L1_conv_g2, L1_conv_b2, L1_conv_m2, L1_conv_v2):
    import jax
    import jax.numpy as jnp
    def _L0_conv_ref(x, negative_dict):
        import jax, jax.numpy as jnp
        import numpy as np
        THRESHOLD = 0.625
        f_norm = x / jnp.linalg.norm(x, axis=1, keepdims=True)
        d_norm = negative_dict / jnp.linalg.norm(negative_dict, axis=1, keepdims=True)
        sim = jnp.einsum('bchw,nc->bnhw', f_norm, d_norm)
        dist = (1.0 - sim) * 0.5
        apm = jnp.min(dist, axis=1, keepdims=True)
        index = jnp.argmin(dist, axis=1)
        replace_map = (apm < THRESHOLD).astype(x.dtype)
        restructured = negative_dict[index]
        restructured = jnp.transpose(restructured, (0, 3, 1, 2))
        out = x * (1.0 - replace_map) + restructured * replace_map
        return out

    def _L1_conv_ref(x, w_dw, w_pw, g1, b1, m1, v1, g2, b2, m2, v2):
        import jax, jax.numpy as jnp
        import numpy as np
        from jax import lax
        B, C, H, W = (32, 512, 56, 56)
        CO = 512
        EPS = 1e-05

        def binarize(x):
            xc = jnp.clip(x, -1.0, 1.0)
            return xc + lax.stop_gradient(jnp.sign(x) - xc)

        def batchnorm(y, g, b, m, v):
            inv = g * lax.rsqrt(v + EPS)
            return y * inv[None, :, None, None] + (b - m * inv)[None, :, None, None]
        dn = ('NCHW', 'OIHW', 'NCHW')
        out = lax.conv_general_dilated(binarize(x), binarize(w_dw), window_strides=(1, 1), padding=((1, 1), (1, 1)), feature_group_count=C, dimension_numbers=dn)
        out = batchnorm(out, g1, b1, m1, v1)
        out = lax.conv_general_dilated(binarize(out), binarize(w_pw), window_strides=(1, 1), padding=((0, 0), (0, 0)), dimension_numbers=dn)
        out = batchnorm(out, g2, b2, m2, v2)
        return out

    def _gn(v, G=32, eps=1e-5):
        B_, C_, H_, W_ = v.shape
        g = v.reshape(B_, G, C_ // G, H_, W_)
        m = jnp.mean(g, axis=(2, 3, 4), keepdims=True)
        s = jnp.var(g, axis=(2, 3, 4), keepdims=True)
        return ((g - m) / jnp.sqrt(s + eps)).reshape(v.shape)

    def _ln_c(v, eps=1e-6):
        m = jnp.mean(v, axis=1, keepdims=True)
        s = jnp.var(v, axis=1, keepdims=True)
        return (v - m) / jnp.sqrt(s + eps)

    def _ln_t(v, eps=1e-5):
        m = jnp.mean(v, axis=-1, keepdims=True)
        s = jnp.var(v, axis=-1, keepdims=True)
        return (v - m) / jnp.sqrt(s + eps)

    def _to_tokens(v):
        B_, C_, H_, W_ = v.shape
        return v.reshape(B_, C_, H_ * W_).transpose(0, 2, 1)
    def _from_tokens(t, like):
        B_, C_, H_, W_ = like.shape
        return t.transpose(0, 2, 1).reshape(B_, C_, H_, W_)

    x = x + _L0_conv_ref(_gn(x), L0_conv_negative_dict)
    x = x + _L1_conv_ref(_gn(x), L1_conv_w_dw, L1_conv_w_pw, L1_conv_g1, L1_conv_b1, L1_conv_m1, L1_conv_v1, L1_conv_g2, L1_conv_b2, L1_conv_m2, L1_conv_v2)
    return x


_drawn_inputs = setup_inputs


def setup_inputs(seed=0):
    import zlib

    import numpy as np

    out = dict(_drawn_inputs(seed))
    spreads = {}
    factors = {'L1_conv_b2': 2.703}
    for name, (base, spread) in spreads.items():
        noise = np.random.default_rng([zlib.crc32(name.encode()), seed]).standard_normal(out[name].shape)
        drawn = base * np.exp(spread * noise) if base else spread * noise
        out[name] = jnp.asarray(drawn.astype(out[name].dtype))
    for name, factor in factors.items():
        out[name] = (out[name] * factor).astype(out[name].dtype)
    return out
```

```python
import concourse.bass as bass
from concourse import mybir
from contextlib import ExitStack

FP32 = mybir.dt.float32
FP16 = mybir.dt.float16
BF16 = mybir.dt.bfloat16
FP8 = mybir.dt.float8e4
U32 = mybir.dt.uint32
I32 = mybir.dt.int32
ALU = mybir.AluOpType
ACT = mybir.ActivationFunctionType
AX = mybir.AxisListType

P = 128
NI, C, H, W = 16, 512, 64, 64
PIX = H * W
KC = C // P
NB = 8
ROWS = H // NB
BP = PIX // NB
NT = BP // P
ND = 512
GROUP = C // 32
GN_EPS = 1e-5
BN_EPS = 1e-5
G_SCALE = 16.0
D_SCALE = 64.0
SQ_SCALE = 0.25
SIM_LIMIT = 1.0 - 2.0 * 0.625
Q_FACTOR = SQ_SCALE ** 2 / (SIM_LIMIT * G_SCALE * D_SCALE) ** 2
STAT_STEPS = 9


def at_least(engine, sem, value):
    if isinstance(value, int) and value <= 0:
        return
    engine.wait_ge(sem, value)


def wait_apart(engine, begun, *waits):
    waits = [(sem, value if isinstance(value, int) else engine.to_reg(value)) for sem, value in waits]
    engine.wait_ge(begun, 1)
    for sem, value in waits:
        at_least(engine, sem, value)


def conv_net(nc, x, dic, w_dw, w_pwT, bn, out):
    x_v = x.rearrange("n (k c) h w -> n c k (h w)", c=P)
    o_v = out.rearrange("n (k c) h w -> n c k (h w)", c=P)
    table = nc.dram_tensor("table", [ND + 1, C], FP32, kind="Internal").ap()

    ctx = ExitStack()
    with ctx:
        def sb(name, shape, dt):
            return ctx.enter_context(nc.sbuf_tensor(name, shape, dt))

        def pb(name, shape, dt):
            return ctx.enter_context(nc.psum_tensor(name, shape, dt))

        def sem(name):
            return ctx.enter_context(nc.semaphore(name))

        X = sb("X", [P, 2, KC, PIX], FP32)
        g_ring = sb("g_ring", [P, 2, BP], FP32)
        g_hi = sb("g_hi", [P, 2, KC, BP], FP16)
        g_lo = sb("g_lo", [P, 2, KC, BP], FP16)
        sq_ring = sb("sq_ring", [P, 2, BP], FP32)
        sq_sum = sb("sq_sum", [P, BP], FP32)
        sq_hi = sb("sq_hi", [P, 2, BP], FP16)
        sq_lo = sb("sq_lo", [P, 2, BP], FP16)
        g_sel = sb("g_sel", [P, 2, BP], FP32)
        rows = sb("rows", [P, 2, NT, C], FP32)
        plane = sb("plane", [P, KC, H + 2, W + 2], FP8)
        mid = sb("mid", [P, 2, KC, BP], FP8)
        dT_hi = sb("dT_hi", [P, KC, ND], FP16)
        dT_lo = sb("dT_lo", [P, KC, ND], FP16)
        pw = sb("pw", [P, KC, C], FP8)
        diag = sb("diag", [P, KC, 9, P], FP8)
        ident = sb("ident", [P, P], FP32)
        ident16 = sb("ident16", [P, P], BF16)
        group_mean = sb("group_mean", [P, P], FP32)
        ones16 = sb("ones16", [P, 1], FP16)
        tops = sb("tops", [P, 2, NT, 8], FP32)
        top_at = sb("top_at", [P, 2, NT, 8], U32)
        n2 = sb("n2", [P, 2, NT], FP32)
        q_min = sb("q_min", [P, NT], FP32)
        taken = sb("taken", [P, NT], FP32)
        kept = sb("kept", [P, 2, NT], BF16)
        row_at = sb("row_at", [P, 2, NT], U32)
        bn6 = sb("bn6", [P, KC, NB, 6], FP32)
        mv = sb("mv", [P, KC, 2], FP32)
        gm = sb("gm", [P, KC], FP32)
        dev = sb("dev", [P, KC], FP32)
        dev2 = sb("dev2", [P, KC], FP32)
        spread = sb("spread", [P, KC], FP32)
        var = sb("var", [P, KC], FP32)
        root = sb("root", [P, KC], FP32)
        quot = sb("quot", [P, KC], FP32)
        std = sb("std", [P, KC], FP32)
        aff = sb("aff", [P, 2, KC], FP32)
        aff_g = sb("aff_g", [P, 2, KC], FP32)
        aff_q = sb("aff_q", [P, 2, KC], FP32)
        x_sums = sb("x_sums", [P, KC, NB], FP32)
        x_sum = sb("x_sum", [P, KC], FP32)
        neg_mean = sb("neg_mean", [P, KC], FP32)
        wd = sb("wd", [P, KC, 9], FP32)
        wds = sb("wds", [P, KC, 9], FP32)
        bnv = sb("bnv", [P, 8, KC], FP32)
        bn_a = sb("bn_a", [P, 2, KC], FP32)
        bn_r = sb("bn_r", [P, 2, KC], FP32)
        bn_q = sb("bn_q", [P, 2, KC], FP32)
        bn_s = sb("bn_s", [P, 2, KC], FP32)
        bn_i = sb("bn_i", [P, 2, KC], FP32)
        bn_m = sb("bn_m", [P, 2, KC], FP32)
        bn_b = sb("bn_b", [P, 2, KC], FP32)
        d_n2 = sb("d_n2", [P, KC], FP32)
        d_r = sb("d_r", [P, KC], FP32)
        d_q = sb("d_q", [P, KC], FP32)
        d_s = sb("d_s", [P, KC], FP32)

        sim = [pb(f"sim{i}", [P, ND], FP32) for i in range(2)]
        back = pb("back", [P, BP], FP32)
        misc = pb("misc", [P, BP], FP32)
        dwp = [pb(f"dwp{i}", [P, BP], FP32) for i in range(2)]
        pwp = [pb(f"pwp{i}", [P, BP], FP32) for i in range(2)]

        dict_rows = rows[:, 0]
        unit_rows = rows[:, 1]
        pw_raw = X[:, 1, 0, 0:KC * C].rearrange("p (k n) -> p k n", k=KC)
        zero_row = g_ring[0:1, 0, :]

        loaded = [sem(f"loaded{b}") for b in range(NB)]
        stored = [sem(f"stored{b}") for b in range(NB)]
        const_in = sem("const_in")
        begun = sem("begun")
        table_in = sem("table_in")
        zero_ok = sem("zero_ok")
        id_ok = sem("id_ok")
        pool_setup = sem("pool_setup")
        act_setup = sem("act_setup")
        act_roots = sem("act_roots")
        act_split = sem("act_split")
        dve_setup = sem("dve_setup")
        dve_split = sem("dve_split")
        pe_setup = sem("pe_setup")
        stat = sem("stat")
        stat_bn = sem("stat_bn")
        stat_mm = sem("stat_mm")
        stat_root = sem("stat_root")
        g_ok = sem("g_ok")
        hi_ok = sem("hi_ok")
        sq_ok = sem("sq_ok")
        lo_ok = sem("lo_ok")
        sq_used = sem("sq_used")
        acc = sem("acc")
        sim_ok = sem("sim_ok")
        top_ok = sem("top_ok")
        top_used = sem("top_used")
        norm_ok = sem("norm_ok")
        norm_used = sem("norm_used")
        pick = sem("pick")
        gathered = [sem(f"gathered{i}") for i in range(2)]
        kept_ok = sem("kept_ok")
        back_ok = sem("back_ok")
        gsel_ok = sem("gsel_ok")
        sel_ok = sem("sel_ok")
        x1_ok = sem("x1_ok")
        mean_step = sem("mean_step")
        mean_mm = sem("mean_mm")
        sign_ok = sem("sign_ok")
        dw_ok = sem("dw_ok")
        mid_ok = sem("mid_ok")
        pw_ok = sem("pw_ok")
        y_ok = sem("y_ok")
        out_ok = sem("out_ok")

        def px(b):
            return slice(b * BP, (b + 1) * BP)

        def cnt(p, b, per, i=0):
            return p * (NB * per) + (b * per + i)

        block = ctx.enter_context(nc.Block())

        @block.sync
        def _(sp):
            def load(p, half, b):
                sp.dma_start(X[:, half, :, px(b)], x_v[p, :, :, px(b)]).then_inc(loaded[b], 16)

            def store(p, half, b):
                at_least(sp, out_ok, 2 + cnt(p, b, KC, KC))
                sp.dma_start(o_v[p, :, :, px(b)], X[:, half, :, px(b)]).then_inc(stored[b], 16)

            def period(p, half, more):
                for b in range(NB + 1):
                    if b < NB:
                        store(p - 1, 1 - half, b)
                    if more and b > 0:
                        at_least(sp, stored[b - 1], 16 * p)
                        load(p + 1, 1 - half, b - 1)

            for b in range(NB):
                load(0, 0, b)
            sp.dma_start(dict_rows, dic.rearrange("(k n) c -> n k c", n=P)).then_inc(const_in, 16)
            sp.dma_start(pw_raw, w_pwT.rearrange("(k c) n -> c k n", c=P)).then_inc(const_in, 16)
            sp.dma_start(wd[:], w_dw.rearrange("(k c) o i j -> c k (o i j)", c=P)).then_inc(const_in, 16)
            for i, v in enumerate(bn):
                sp.dma_start(bnv[:, i, :], v).then_inc(const_in, 16)
            sp.dma_start(table[1:ND + 1, :], dic).then_inc(table_in, 16)
            sp.wait_ge(zero_ok, 1)
            sp.dma_start(table[0:1, :], zero_row).then_inc(table_in, 16)
            sp.wait_ge(dve_setup, 6)
            for b in range(NB):
                load(1, 1, b)
            with sp.Fori(0, NI // 2 - 1) as pair:
                p = pair * 2 + 1
                period(p, 1, True)
                period(p + 1, 0, True)
            period(NI - 1, 1, False)
            period(NI, 0, False)
            for b in range(NB):
                sp.wait_ge(stored[b], 16 * NI)

        @block.gpsimd
        def _(pool):
            pool.memset(g_ring[:, 0, :], 0.0).then_inc(zero_ok, 1)
            pool.sem_inc(begun, 1)
            pool.memset(ident[:], 0.0).then_inc(id_ok, 1)
            pool.memset(group_mean[:], 1.0 / GROUP).then_inc(id_ok, 1)
            pool.memset(ones16[:], 1.0).then_inc(pool_setup, 1)
            pool.memset(plane[:], 0.0).then_inc(pool_setup, 1)
            pool.wait_ge(id_ok, 2)
            pool.affine_select(out=ident[:], in_=ident[:], compare_op=ALU.not_equal, fill=1.0, base=0,
                               pattern=[[-1, P]], channel_multiplier=1).then_inc(id_ok, 1)
            gv = group_mean[:].rearrange("p (a c) -> p a c", c=GROUP)
            pool.affine_select(out=gv, in_=gv, compare_op=ALU.is_ge, fill=0.0, base=0,
                               pattern=[[-GROUP, P // GROUP], [0, GROUP]],
                               channel_multiplier=1).then_inc(id_ok, 1)
            pool.wait_ge(id_ok, 4)
            pool.tensor_copy(ident16[:], ident[:]).then_inc(pool_setup, 1)
            pool.affine_select(out=gv, in_=gv, compare_op=ALU.is_ge, fill=0.0, base=GROUP - 1,
                               pattern=[[GROUP, P // GROUP], [0, GROUP]],
                               channel_multiplier=-1).then_inc(pool_setup, 1)

            def prepare(p, b):
                s = b % 2
                for k in range(KC):
                    pool.wait_ge(g_ok, cnt(p, b, KC, k + 1))
                    pool.wait_ge(hi_ok, cnt(p, b, KC, k + 1))
                    pool.tensor_tensor(g_lo[:, s, k], g_ring[:, k % 2], g_hi[:, s, k],
                                       ALU.subtract).then_inc(lo_ok, 1)
                    if k == 0:
                        continue
                    pool.wait_ge(sq_ok, cnt(p, b, KC, k + 1))
                    at_least(pool, acc, cnt(p, b, 5, k - 1))
                    pool.tensor_tensor(sq_sum[:], sq_ring[:, 0] if k == 1 else sq_sum[:],
                                       sq_ring[:, k % 2], ALU.add).then_inc(acc, 1)
                wait_apart(pool, begun, (acc, cnt(p, b, 5, 3)))
                pool.tensor_copy(sq_hi[:, s], sq_sum[:]).then_inc(acc, 1)
                pool.wait_ge(acc, cnt(p, b, 5, 4))
                pool.tensor_tensor(sq_lo[:, s], sq_sum[:], sq_hi[:, s], ALU.subtract).then_inc(acc, 1)

            def gather(p, b):
                s = b % 2
                wait_apart(pool, begun, (pick, cnt(p, b, 4, 4)),
                                        (back_ok, cnt(p, b - 1, KC)))
                for t in range(NT):
                    pool.indirect_dma_start(rows[:, s, t, :], None, table[:, :],
                                            bass.IndirectOffsetOnAxis(row_at[:, s, t:t + 1], 0)
                                            ).then_inc(gathered[s], 16)

            def period(p):
                prepare(p, 0)
                for j in range(NB // 2):
                    prepare(p, 2 * j + 1)
                    gather(p, 2 * j)
                    if 2 * j + 2 < NB:
                        prepare(p, 2 * j + 2)
                    gather(p, 2 * j + 1)

            pool.wait_ge(table_in, 32)
            pool.wait_ge(pe_setup, 4)
            period(0)
            with pool.Fori(0, NI // 2 - 1) as pair:
                p = pair * 2 + 1
                period(p)
                period(p + 1)
            period(NI - 1)

        @block.scalar
        def _(act):
            a = nc.scalar
            act.wait_ge(const_in, 16 * 11)
            for k in range(KC):
                a.activation(X[:, 1, 1, px(k)], dict_rows[:, k], ACT.Square,
                             accum_out=d_n2[:, k:k + 1]).then_inc(act_setup, 1)
            a.activation(wds[:], wd[:], ACT.Sign).then_inc(act_setup, 1)
            a.activation(pw[:], pw_raw, ACT.Sign, saturate=False).then_inc(act_setup, 1)
            act.wait_ge(act_setup, KC)
            a.activation(d_r[:], d_n2[:], ACT.Sqrt).then_inc(act_roots, 1)
            act.wait_ge(dve_setup, 1)
            a.activation(bn_r[:], bn_a[:], ACT.Sqrt).then_inc(act_roots, 1)
            for k in range(KC):
                act.wait_ge(pe_setup, k + 1)
                a.activation(dT_hi[:, k], sim[k % 2][:], ACT.Copy).then_inc(act_split, 1)

            def root_of_variance(p):
                act.wait_ge(stat, p * STAT_STEPS + 4)
                a.activation(root[:], var[:], ACT.Sqrt).then_inc(stat_root, 1)

            def split(p, half, b, k):
                s = b % 2
                at_least(act, sim_ok, cnt(p, b - 1, NT))
                at_least(act, norm_ok, cnt(p, b - 1, 1))
                xv = X[:, half, k, px(b)]
                a.activation(g_hi[:, s, k], xv, ACT.Identity, bias=aff_g[:, 1, k:k + 1],
                             scale=aff_g[:, 0, k:k + 1]).then_inc(hi_ok, 1)
                if k >= 2:
                    act.wait_ge(acc, cnt(p, b, 5, 1))
                else:
                    at_least(act, acc, cnt(p, b - 1, 5, 3))
                a.activation(sq_ring[:, k % 2], xv, ACT.Square, bias=aff_q[:, 1, k:k + 1],
                             scale=aff_q[:, 0, k:k + 1]).then_inc(sq_ok, 1)

            def g_again(p, half, b, k):
                at_least(act, sel_ok, cnt(p, b, KC, k - 1))
                a.activation(g_sel[:, k % 2], X[:, half, k, px(b)], ACT.Identity,
                             bias=aff[:, 1, k:k + 1], scale=aff[:, 0, k:k + 1]).then_inc(gsel_ok, 1)

            def signs(q, half, b):
                wait_apart(act, begun, (mean_step, 2 * q + 2 if b == 0 else 0))
                for k in range(KC):
                    ins = a.activation(plane[:, k, 1 + b * ROWS:1 + (b + 1) * ROWS, 1:1 + W],
                                       X[:, half, k, px(b)].rearrange("p (h w) -> p h w", w=W),
                                       ACT.Sign, bias=neg_mean[:, k:k + 1], scale=1.0,
                                       saturate=False)
                ins.then_inc(sign_ok, 1)

            def mids(q, b, k):
                wait_apart(act, begun, (dw_ok, cnt(q, b, KC, k + 1)),
                                       (pw_ok, cnt(q, b - 1, KC) if b >= 2 else 0))
                a.activation(mid[:, b % 2, k], dwp[k % 2][:], ACT.Sign, bias=bn_b[:, 0, k:k + 1],
                             scale=bn_i[:, 0, k:k + 1], saturate=False).then_inc(mid_ok, 1)

            def second_norm(q, b):
                for k in range(KC):
                    act.wait_ge(pw_ok, cnt(q, b, KC, k + 1))
                    a.activation(pwp[k % 2][:], pwp[k % 2][:], ACT.Identity, bias=bn_b[:, 1, k:k + 1],
                                 scale=bn_i[:, 1, k:k + 1]).then_inc(y_ok, 1)

            def period(p, half, match, conv):
                q, old = p - 1, 1 - half
                if conv:
                    signs(q, old, 0)
                    signs(q, old, 1)
                    for k in range(KC):
                        mids(q, 0, k)
                    signs(q, old, 2)
                    second_norm(q, 0)
                    for k in range(KC):
                        mids(q, 1, k)
                if match:
                    root_of_variance(p)
                    act.wait_ge(stat, p * STAT_STEPS + 9)
                    for k in range(KC):
                        split(p, half, 0, k)
                if conv:
                    signs(q, old, 3)
                    second_norm(q, 1)
                for j in range(NB // 2):
                    b = 2 * j
                    if match:
                        for k in range(KC):
                            split(p, half, b + 1, k)
                        if j:
                            g_again(p, half, b - 1, 0)
                            g_again(p, half, b - 1, 1)
                    for k in range(KC):
                        if conv:
                            mids(q, 2 + j, k)
                        if match and j and k < 2:
                            g_again(p, half, b - 1, 2 + k)
                    if match:
                        g_again(p, half, b, 0)
                        g_again(p, half, b, 1)
                        if b + 2 < NB:
                            split(p, half, b + 2, 0)
                            split(p, half, b + 2, 1)
                        g_again(p, half, b, 2)
                        if b + 2 < NB:
                            split(p, half, b + 2, 2)
                            split(p, half, b + 2, 3)
                        g_again(p, half, b, 3)
                    if conv:
                        if 4 + j < NB:
                            signs(q, old, 4 + j)
                        second_norm(q, 2 + j)
                if match:
                    g_again(p, half, NB - 1, 0)
                    g_again(p, half, NB - 1, 1)
                for k in range(KC):
                    if conv:
                        mids(q, 6, k)
                    if match and k < 2:
                        g_again(p, half, NB - 1, 2 + k)
                if conv:
                    second_norm(q, 6)
                    for k in range(KC):
                        mids(q, 7, k)
                    second_norm(q, 7)

            act.wait_ge(pool_setup, 4)
            act.wait_ge(dve_setup, 5)
            period(0, 0, True, False)
            with act.Fori(0, NI // 2 - 1) as pair:
                p = pair * 2 + 1
                period(p, 1, True, True)
                period(p + 1, 0, True, True)
            period(NI - 1, 1, True, True)
            period(NI, 0, False, True)

        @block.vector
        def _(dve):
            v = nc.vector

            dve.wait_ge(const_in, 16 * 11)
            eps_in = bnv[:, 3:8:4, :]
            v.tensor_scalar(bn_a[:], eps_in, BN_EPS, None, ALU.add).then_inc(dve_setup, 1)
            dve.wait_ge(act_roots, 1)
            own = sem("own")
            steps = [0]

            def then(ins):
                steps[0] += 1
                ins.then_inc(own, 1)
                dve.wait_ge(own, steps[0])

            then(v.reciprocal(d_q[:], d_r[:]))
            then(v.tensor_tensor(d_q[:], d_n2[:], d_q[:], ALU.mult))
            then(v.tensor_tensor(d_s[:], d_q[:], d_r[:], ALU.add))
            then(v.reciprocal(d_s[:], d_s[:]))
            for k in range(KC):
                last = v.tensor_scalar(unit_rows[:, k], dict_rows[:, k], d_s[:, k:k + 1], 2 * D_SCALE,
                                       ALU.mult, ALU.mult)
            last.then_inc(dve_setup, 1)
            dve.wait_ge(act_roots, 2)
            then(v.reciprocal(bn_q[:], bn_r[:]))
            then(v.tensor_tensor(bn_q[:], bn_a[:], bn_q[:], ALU.mult))
            then(v.tensor_tensor(bn_s[:], bn_q[:], bn_r[:], ALU.add))
            then(v.reciprocal(bn_s[:], bn_s[:]))
            then(v.scalar_tensor_tensor(bn_i[:], bnv[:, 0:5:4, :], 2.0, bn_s[:], ALU.mult, ALU.mult))
            then(v.tensor_tensor(bn_m[:], bnv[:, 2:7:4, :], bn_i[:], ALU.mult))
            v.tensor_tensor(bn_b[:], bnv[:, 1:6:4, :], bn_m[:], ALU.subtract).then_inc(dve_setup, 1)
            dve.wait_ge(pool_setup, 4)
            dve.wait_ge(act_setup, KC + 1)
            for k in range(KC):
                for tap in range(9):
                    last = v.tensor_scalar(diag[:, k, tap], ident16[:], wds[:, k, tap:tap + 1], None,
                                           ALU.mult, saturate=False)
            last.then_inc(dve_setup, 1)
            for k in range(KC):
                dve.wait_ge(act_split, k + 1)
                v.tensor_tensor(dT_lo[:, k], sim[k % 2][:], dT_hi[:, k], ALU.subtract).then_inc(dve_split, 1)
            dve.wait_ge(act_setup, KC + 2)
            v.memset(x_sums[:], 0.0).then_inc(dve_setup, 2)
            v.memset(q_min[:], 0.0).then_inc(out_ok, 2)

            def block_stats(p, half, b):
                wait_apart(dve, begun, (loaded[b], 16 * (p + 1)))
                for k in range(KC):
                    ins = v.bn_stats(bn6[:, k, b, :], X[:, half, k, px(b)])
                ins.then_inc(stat_bn, 1)

            def group_norm(p):
                n = p * STAT_STEPS
                wait_apart(dve, begun, (stat_bn, NB * (p + 1)))
                for k in range(KC):
                    ins = v.bn_aggr(mv[:, k, :], bn6[:, k, :, :])
                ins.then_inc(stat, 1)
                dve.wait_ge(stat, n + 1)
                dve.wait_ge(stat_mm, 2 * p + 1)
                v.tensor_copy(gm[:], misc[:, 0:KC])
                v.tensor_tensor(dev[:], mv[:, :, 0], misc[:, 0:KC], ALU.subtract).then_inc(stat, 1)
                dve.wait_ge(stat, n + 2)
                v.tensor_tensor(dev2[:], dev[:], dev[:], ALU.mult).then_inc(stat_own, 1)
                dve.wait_ge(stat_own, 4 * p + 1)
                v.tensor_tensor(spread[:], dev2[:], mv[:, :, 1], ALU.add).then_inc(stat, 1)
                dve.wait_ge(stat_mm, 2 * p + 2)
                v.tensor_scalar(var[:], misc[:, KC:2 * KC], GN_EPS, None, ALU.add).then_inc(stat, 1)
                dve.wait_ge(stat, n + 4)
                dve.wait_ge(stat_root, p + 1)
                v.reciprocal(quot[:], root[:]).then_inc(stat_own, 1)
                dve.wait_ge(stat_own, 4 * p + 2)
                v.tensor_tensor(quot[:], var[:], quot[:], ALU.mult).then_inc(stat, 1)
                dve.wait_ge(stat, n + 5)
                v.tensor_tensor(std[:], quot[:], root[:], ALU.add).then_inc(stat, 1)
                dve.wait_ge(stat, n + 6)
                v.reciprocal(dev[:], std[:]).then_inc(stat_own, 1)
                dve.wait_ge(stat_own, 4 * p + 3)
                v.tensor_scalar(aff[:, 0, :], dev[:], 2.0, None, ALU.mult).then_inc(stat, 1)
                dve.wait_ge(stat, n + 7)
                v.scalar_tensor_tensor(aff[:, 1, :], gm[:], -1.0, aff[:, 0, :], ALU.mult,
                                       ALU.mult).then_inc(stat_own, 1)
                dve.wait_ge(stat_own, 4 * p + 4)
                v.tensor_scalar(aff_g[:], aff[:], G_SCALE, None, ALU.mult).then_inc(stat, 1)
                v.tensor_scalar(aff_q[:], aff[:], SQ_SCALE, None, ALU.mult).then_inc(stat, 1)
                dve.wait_ge(stat, n + 9)

            def norm_block(p, half, b):
                for k in range(KC):
                    if k >= 2:
                        dve.wait_ge(lo_ok, cnt(p, b, KC, k - 1))
                    else:
                        at_least(dve, lo_ok, cnt(p, b, KC, k - 1))
                    v.tensor_scalar(g_ring[:, k % 2], X[:, half, k, px(b)], gm[:, k:k + 1],
                                    aff_g[:, 0, k:k + 1], ALU.subtract, ALU.mult).then_inc(g_ok, 1)

            def take_norm(p, b):
                dve.wait_ge(norm_ok, cnt(p, b, 1, 1))
                v.tensor_copy(n2[:, b % 2], misc[:, 0:NT]).then_inc(norm_used, 1)

            def top(p, b, t):
                s = b % 2
                wait_apart(dve, begun, (sim_ok, cnt(p, b, NT, t + 1)))
                v.max(tops[:, s, t], sim[t % 2][:]).then_inc(top_ok, 1)
                wait_apart(dve, begun, (top_ok, cnt(p, b, NT, t + 1)))
                v.max_index(top_at[:, s, t], tops[:, s, t], sim[t % 2][:]).then_inc(top_used, 1)

            def choose(p, b):
                s = b % 2
                m = tops[:, s, :, 0]
                dve.wait_ge(top_used, cnt(p, b, NT, NT))
                dve.wait_ge(norm_used, cnt(p, b, 1, 1))
                v.scalar_tensor_tensor(q_min[:], m, 0.0, m, ALU.min, ALU.mult).then_inc(pick, 1)
                dve.wait_ge(pick, cnt(p, b, 4, 1))
                v.scalar_tensor_tensor(taken[:], q_min[:], Q_FACTOR, n2[:, s], ALU.mult,
                                       ALU.is_lt).then_inc(pick, 1)
                dve.wait_ge(pick, cnt(p, b, 4, 2))
                v.tensor_scalar(kept[:, s], taken[:], -1.0, 1.0, ALU.mult, ALU.add).then_inc(pick, 1)
                v.scalar_tensor_tensor(row_at[:, s], top_at[:, s, :, 0], 1.0, taken[:], ALU.add,
                                       ALU.mult).then_inc(pick, 1)

            def residual(p, half, b, k):
                wait_apart(dve, begun, (kept_ok, cnt(p, b, 1, 1)),
                                       (gsel_ok, cnt(p, b, KC, k + 1)),
                                       (back_ok, cnt(p, b, KC, k + 1)))
                v.copy_predicated(back[:], misc[:].bitcast(I32), g_sel[:, k % 2]).then_inc(sel_ok, 1)
                dve.wait_ge(sel_ok, cnt(p, b, KC, k + 1))
                xv = X[:, half, k, px(b)]
                v.scalar_tensor_tensor(xv, back[:], 1.0, xv, ALU.mult, ALU.add,
                                       accum_out=x_sums[:, k, b:b + 1]).then_inc(x1_ok, 1)

            def finish(q, half, b):
                for k in range(KC):
                    dve.wait_ge(y_ok, cnt(q, b, KC, k + 1))
                    xv = X[:, half, k, px(b)]
                    v.tensor_tensor(xv, pwp[k % 2][:], xv, ALU.add).then_inc(out_ok, 1)

            def period(p, half, match, conv, stats):
                q, old = p - 1, 1 - half
                if conv:
                    finish(q, old, 0)
                if match:
                    if conv:
                        block_stats(p, half, 6)
                        block_stats(p, half, 7)
                    group_norm(p)
                    norm_block(p, half, 0)
                if conv:
                    finish(q, old, 1)
                for j in range(NB // 2):
                    b = 2 * j
                    if match:
                        norm_block(p, half, b + 1)
                        take_norm(p, b)
                        for t in range(NT):
                            top(p, b, t)
                        choose(p, b)
                        if j:
                            for k in range(KC):
                                residual(p, half, b - 1, k)
                        if b + 2 < NB:
                            norm_block(p, half, b + 2)
                        take_norm(p, b + 1)
                        top(p, b + 1, 0)
                        top(p, b + 1, 1)
                        residual(p, half, b, 0)
                        top(p, b + 1, 2)
                        residual(p, half, b, 1)
                        top(p, b + 1, 3)
                        choose(p, b + 1)
                        residual(p, half, b, 2)
                        residual(p, half, b, 3)
                    if conv:
                        finish(q, old, 2 + j)
                    if stats:
                        block_stats(p + 1, old, j)
                if match:
                    for k in range(KC):
                        residual(p, half, NB - 1, k)
                    dve.wait_ge(x1_ok, cnt(p, NB, KC))
                    at_least(dve, sign_ok, NB * p)
                    v.reduce_sum(x_sum[:], x_sums[:], AX.X).then_inc(mean_step, 1)
                if conv:
                    finish(q, old, 6)
                if match:
                    dve.wait_ge(mean_mm, p + 1)
                    v.tensor_scalar(neg_mean[:], misc[:, 0:KC], -1.0 / PIX, None,
                                    ALU.mult).then_inc(mean_step, 1)
                if stats:
                    block_stats(p + 1, old, 4)
                if conv:
                    finish(q, old, 7)
                if stats:
                    block_stats(p + 1, old, 5)

            stat_own = sem("stat_own")
            dve.wait_ge(table_in, 32)
            for b in range(NB):
                block_stats(0, 0, b)
            period(0, 0, True, False, True)
            with dve.Fori(0, NI // 2 - 1) as pair:
                p = pair * 2 + 1
                period(p, 1, True, True, True)
                period(p + 1, 0, True, True, True)
            period(NI - 1, 1, True, True, False)
            period(NI, 0, False, True, False)

        @block.tensor
        def _(pe):
            t_ = nc.tensor
            pe.wait_ge(pool_setup, 4)
            pe.wait_ge(dve_setup, 2)
            for k in range(KC):
                if k >= 2:
                    pe.wait_ge(dve_split, k - 1)
                for n in range(KC):
                    last = t_.transpose(sim[k % 2][:, n * P:(n + 1) * P],
                                        unit_rows[:, n, k * P:(k + 1) * P], ident[:])
                last.then_inc(pe_setup, 1)
            pe.wait_ge(dve_split, KC)
            pe.wait_ge(dve_setup, 6)

            def means(p):
                pe.wait_ge(stat, p * STAT_STEPS + 1)
                t_.matmul(misc[:, 0:KC], group_mean[:], mv[:, :, 0], start=True,
                          stop=True).then_inc(stat_mm, 1)

            def spreads(p):
                pe.wait_ge(stat, p * STAT_STEPS + 3)
                t_.matmul(misc[:, KC:2 * KC], group_mean[:], spread[:], start=True,
                          stop=True).then_inc(stat_mm, 1)

            def norms(p, b):
                s = b % 2
                pe.wait_ge(acc, cnt(p, b, 5, 5))
                at_least(pe, x1_ok, cnt(p, b - 1, KC))
                if b == 0:
                    pe.wait_ge(stat, p * STAT_STEPS + 4)
                for t in range(NT):
                    px_t = slice(t * P, (t + 1) * P)
                    t_.matmul(misc[:, t:t + 1], sq_hi[:, s, px_t], ones16[:], start=True, stop=False)
                    last = t_.matmul(misc[:, t:t + 1], sq_lo[:, s, px_t], ones16[:], start=False,
                                     stop=True)
                last.then_inc(norm_ok, 1)

            def products(p, b, t):
                s = b % 2
                if t == 0:
                    pe.wait_ge(hi_ok, cnt(p, b, KC, KC))
                    pe.wait_ge(lo_ok, cnt(p, b, KC, KC))
                at_least(pe, top_used, cnt(p, b, NT, t - 1))
                px_t = slice(t * P, (t + 1) * P)
                for k in range(KC):
                    t_.matmul(sim[t % 2][:], g_hi[:, s, k, px_t], dT_hi[:, k], start=(k == 0), stop=False)
                    t_.matmul(sim[t % 2][:], g_hi[:, s, k, px_t], dT_lo[:, k], start=False, stop=False)
                    last = t_.matmul(sim[t % 2][:], g_lo[:, s, k, px_t], dT_hi[:, k], start=False,
                                     stop=(k == KC - 1))
                last.then_inc(sim_ok, 1)

            def spread_kept(p, b):
                s = b % 2
                pe.wait_ge(pick, cnt(p, b, 4, 3))
                at_least(pe, sel_ok, cnt(p, b, KC))
                pe.wait_ge(norm_used, cnt(p, min(b + 1, NB - 1), 1, 1))
                for t in range(NT):
                    last = t_.matmul(misc[:, t * P:(t + 1) * P],
                                     kept[:, s, t:t + 1].to_broadcast([P, P]), ident16[:],
                                     start=True, stop=True)
                last.then_inc(kept_ok, 1)

            def transpose_back(p, b, k):
                s = b % 2
                if k == 0:
                    spread_kept(p, b)
                    pe.wait_ge(gathered[s], p * (16 * NT * NB // 2) + 16 * NT * (b // 2 + 1))
                at_least(pe, x1_ok, cnt(p, b, KC, k))
                for t in range(NT):
                    last = t_.transpose(back[:, t * P:(t + 1) * P], rows[:, s, t, k * P:(k + 1) * P],
                                        ident[:])
                last.then_inc(back_ok, 1)

            def stream_mean(p):
                pe.wait_ge(mean_step, 2 * p + 1)
                t_.matmul(misc[:, 0:KC], group_mean[:], x_sum[:], start=True,
                          stop=True).then_inc(mean_mm, 1)

            def depthwise(q, b, k):
                wait_apart(pe, begun, (sign_ok, q * NB + min(b + 2, NB) if k == 0 else 0),
                                      (mid_ok, cnt(q, b, KC, k - 1) if b or k >= 2 else 0))
                for tap in range(9):
                    dy, dx = tap // 3, tap % 3
                    last = t_.matmul(dwp[k % 2][:], diag[:, k, tap],
                                     plane[:, k, b * ROWS + dy:b * ROWS + dy + ROWS, dx:dx + W],
                                     start=(tap == 0), stop=(tap == 8))
                last.then_inc(dw_ok, 1)

            def pointwise(q, b, n):
                wait_apart(pe, begun, (mid_ok, cnt(q, b, KC, KC) if n == 0 else 0),
                                      (out_ok, cnt(q, b, KC, n + 1)))
                for k in range(KC):
                    last = t_.matmul(pwp[n % 2][:], pw[:, k, n * P:(n + 1) * P], mid[:, b % 2, k],
                                     start=(k == 0), stop=(k == KC - 1))
                last.then_inc(pw_ok, 1)

            def period(p, match, conv):
                q = p - 1
                if conv:
                    for k in range(KC):
                        depthwise(q, 0, k)
                    for n in range(KC):
                        pointwise(q, 0, n)
                    depthwise(q, 1, 0)
                    depthwise(q, 1, 1)
                if match:
                    means(p)
                    spreads(p)
                if conv:
                    depthwise(q, 1, 2)
                    depthwise(q, 1, 3)
                    for n in range(KC):
                        pointwise(q, 1, n)
                for j in range(NB // 2):
                    b = 2 * j
                    if match:
                        norms(p, b)
                        for t in range(NT):
                            products(p, b, t)
                    for k in range(KC):
                        if conv:
                            depthwise(q, 2 + j, k)
                        if match and j:
                            transpose_back(p, b - 1, k)
                    if match:
                        norms(p, b + 1)
                        products(p, b + 1, 0)
                        products(p, b + 1, 1)
                        transpose_back(p, b, 0)
                        products(p, b + 1, 2)
                        transpose_back(p, b, 1)
                        products(p, b + 1, 3)
                        transpose_back(p, b, 2)
                        transpose_back(p, b, 3)
                    if conv:
                        for n in range(KC):
                            pointwise(q, 2 + j, n)
                for k in range(KC):
                    if conv:
                        depthwise(q, 6, k)
                    if match:
                        transpose_back(p, NB - 1, k)
                if conv:
                    for n in range(KC):
                        pointwise(q, 6, n)
                    depthwise(q, 7, 0)
                if match:
                    stream_mean(p)
                if conv:
                    for k in range(1, KC):
                        depthwise(q, 7, k)
                    for n in range(KC):
                        pointwise(q, 7, n)

            period(0, True, False)
            with pe.Fori(0, NI // 2 - 1) as pair:
                p = pair * 2 + 1
                period(p, True, True)
                period(p + 1, True, True)
            period(NI - 1, True, True)
            period(NI, False, True)


def kernel(**inputs):
    import numpy as _np
    import concourse.bacc as _bacc
    from concourse import mybir as _mybir
    from concourse.bass_utils import run_bass_kernel_spmd as _run

    nc = _bacc.Bacc("TRN2", target_bir_lowering=False, num_devices=1, dynamic_dma_scratch_size=4096)
    arrays, args = {}, {}
    for name, value in inputs.items():
        a = _np.asarray(value)
        if name == "L1_conv_w_pw":
            a = a.reshape(C, C).transpose(1, 0)
        elif a.shape == (C,):
            a = a.reshape(KC, P).transpose(1, 0)
        a = _np.ascontiguousarray(a)
        arrays[f"in_{name}"] = a
        args[name] = nc.dram_tensor(f"in_{name}", a.shape, _mybir.dt.from_np(a.dtype),
                                    kind="ExternalInput").ap()
    out = nc.dram_tensor("out_0", (NI, C, H, W), FP32, kind="ExternalOutput").ap()
    bn = [args[f"L1_conv_{v}{i}"] for i in (1, 2) for v in "gbmv"]
    conv_net(nc, args["x"], args["L0_conv_negative_dict"], args["L1_conv_w_dw"], args["L1_conv_w_pw"],
             bn, out)
    r = _run(nc, [arrays], core_ids=[0])
    return r.results[0]["out_0"]
```

```python
import concourse.bass as bass
from concourse import mybir
from contextlib import ExitStack

FP32 = mybir.dt.float32
FP16 = mybir.dt.float16
BF16 = mybir.dt.bfloat16
FP8 = mybir.dt.float8e4
U32 = mybir.dt.uint32
I32 = mybir.dt.int32
ALU = mybir.AluOpType
ACT = mybir.ActivationFunctionType
AX = mybir.AxisListType

P = 128
NI, C, H, W = 16, 512, 64, 64
PIX = H * W
KC = C // P
NB = 8
ROWS = H // NB
BP = PIX // NB
NT = BP // P
ND = 512
GROUP = C // 32
GN_EPS = 1e-5
BN_EPS = 1e-5
G_SCALE = 16.0
D_SCALE = 64.0
SQ_SCALE = 0.25
SIM_LIMIT = 1.0 - 2.0 * 0.625
Q_FACTOR = SQ_SCALE ** 2 / (SIM_LIMIT * G_SCALE * D_SCALE) ** 2
STAT_STEPS = 9


def at_least(engine, sem, value):
    if isinstance(value, int) and value <= 0:
        return
    engine.wait_ge(sem, value)


def wait_apart(engine, begun, *waits):
    waits = [(sem, value if isinstance(value, int) else engine.to_reg(value)) for sem, value in waits]
    engine.wait_ge(begun, 1)
    for sem, value in waits:
        at_least(engine, sem, value)


def conv_net(nc, x, dic, w_dw, w_pwT, bn, out):
    x_v = x.rearrange("n (k c) h w -> n c k (h w)", c=P)
    o_v = out.rearrange("n (k c) h w -> n c k (h w)", c=P)
    table = nc.dram_tensor("table", [ND + 1, C], FP32, kind="Internal").ap()

    ctx = ExitStack()
    with ctx:
        def sb(name, shape, dt):
            return ctx.enter_context(nc.sbuf_tensor(name, shape, dt))

        def pb(name, shape, dt):
            return ctx.enter_context(nc.psum_tensor(name, shape, dt))

        def sem(name):
            return ctx.enter_context(nc.semaphore(name))

        X = sb("X", [P, 2, KC, PIX], FP32)
        g_ring = sb("g_ring", [P, 2, BP], FP32)
        g_hi = sb("g_hi", [P, 2, KC, BP], FP16)
        g_lo = sb("g_lo", [P, 2, KC, BP], FP16)
        sq_ring = sb("sq_ring", [P, 2, BP], FP32)
        sq_sum = sb("sq_sum", [P, BP], FP32)
        sq_hi = sb("sq_hi", [P, 2, BP], FP16)
        sq_lo = sb("sq_lo", [P, 2, BP], FP16)
        g_sel = sb("g_sel", [P, 2, BP], FP32)
        rows = sb("rows", [P, 2, NT, C], FP32)
        plane = sb("plane", [P, KC, H + 2, W + 2], FP8)
        mid = sb("mid", [P, 2, KC, BP], FP8)
        dT_hi = sb("dT_hi", [P, KC, ND], FP16)
        dT_lo = sb("dT_lo", [P, KC, ND], FP16)
        pw = sb("pw", [P, KC, C], FP8)
        diag = sb("diag", [P, KC, 9, P], FP8)
        ident = sb("ident", [P, P], FP32)
        ident16 = sb("ident16", [P, P], BF16)
        group_mean = sb("group_mean", [P, P], FP32)
        ones16 = sb("ones16", [P, 1], FP16)
        tops = sb("tops", [P, 2, NT, 8], FP32)
        top_at = sb("top_at", [P, 2, NT, 8], U32)
        n2 = sb("n2", [P, 2, NT], FP32)
        q_min = sb("q_min", [P, NT], FP32)
        taken = sb("taken", [P, NT], FP32)
        kept = sb("kept", [P, 2, NT], BF16)
        row_at = sb("row_at", [P, 2, NT], U32)
        bn6 = sb("bn6", [P, KC, NB, 6], FP32)
        mv = sb("mv", [P, KC, 2], FP32)
        gm = sb("gm", [P, KC], FP32)
        dev = sb("dev", [P, KC], FP32)
        dev2 = sb("dev2", [P, KC], FP32)
        spread = sb("spread", [P, KC], FP32)
        var = sb("var", [P, KC], FP32)
        root = sb("root", [P, KC], FP32)
        quot = sb("quot", [P, KC], FP32)
        std = sb("std", [P, KC], FP32)
        aff = sb("aff", [P, 2, KC], FP32)
        aff_g = sb("aff_g", [P, 2, KC], FP32)
        aff_q = sb("aff_q", [P, 2, KC], FP32)
        x_sums = sb("x_sums", [P, KC, NB], FP32)
        x_sum = sb("x_sum", [P, KC], FP32)
        neg_mean = sb("neg_mean", [P, KC], FP32)
        wd = sb("wd", [P, KC, 9], FP32)
        wds = sb("wds", [P, KC, 9], FP32)
        bnv = sb("bnv", [P, 8, KC], FP32)
        bn_a = sb("bn_a", [P, 2, KC], FP32)
        bn_r = sb("bn_r", [P, 2, KC], FP32)
        bn_q = sb("bn_q", [P, 2, KC], FP32)
        bn_s = sb("bn_s", [P, 2, KC], FP32)
        bn_i = sb("bn_i", [P, 2, KC], FP32)
        bn_m = sb("bn_m", [P, 2, KC], FP32)
        bn_b = sb("bn_b", [P, 2, KC], FP32)
        d_n2 = sb("d_n2", [P, KC], FP32)
        d_r = sb("d_r", [P, KC], FP32)
        d_q = sb("d_q", [P, KC], FP32)
        d_s = sb("d_s", [P, KC], FP32)

        sim = [pb(f"sim{i}", [P, ND], FP32) for i in range(2)]
        back = pb("back", [P, BP], FP32)
        misc = pb("misc", [P, BP], FP32)
        dwp = [pb(f"dwp{i}", [P, BP], FP32) for i in range(2)]
        pwp = [pb(f"pwp{i}", [P, BP], FP32) for i in range(2)]

        dict_rows = rows[:, 0]
        unit_rows = rows[:, 1]
        pw_raw = X[:, 1, 0, 0:KC * C].rearrange("p (k n) -> p k n", k=KC)
        zero_row = g_ring[0:1, 0, :]

        loaded = [sem(f"loaded{b}") for b in range(NB)]
        stored = [sem(f"stored{b}") for b in range(NB)]
        const_in = sem("const_in")
        begun = sem("begun")
        table_in = sem("table_in")
        zero_ok = sem("zero_ok")
        id_ok = sem("id_ok")
        pool_setup = sem("pool_setup")
        act_setup = sem("act_setup")
        act_roots = sem("act_roots")
        act_split = sem("act_split")
        dve_setup = sem("dve_setup")
        dve_split = sem("dve_split")
        pe_setup = sem("pe_setup")
        stat = sem("stat")
        stat_bn = sem("stat_bn")
        stat_mm = sem("stat_mm")
        stat_root = sem("stat_root")
        g_ok = sem("g_ok")
        hi_ok = sem("hi_ok")
        sq_ok = sem("sq_ok")
        lo_ok = sem("lo_ok")
        sq_used = sem("sq_used")
        acc = sem("acc")
        sim_ok = sem("sim_ok")
        top_ok = sem("top_ok")
        top_used = sem("top_used")
        norm_ok = sem("norm_ok")
        norm_used = sem("norm_used")
        pick = sem("pick")
        gathered = [sem(f"gathered{i}") for i in range(2)]
        kept_ok = sem("kept_ok")
        back_ok = sem("back_ok")
        gsel_ok = sem("gsel_ok")
        sel_ok = sem("sel_ok")
        x1_ok = sem("x1_ok")
        mean_step = sem("mean_step")
        mean_mm = sem("mean_mm")
        sign_ok = sem("sign_ok")
        dw_ok = sem("dw_ok")
        mid_ok = sem("mid_ok")
        pw_ok = sem("pw_ok")
        y_ok = sem("y_ok")
        out_ok = sem("out_ok")

        def px(b):
            return slice(b * BP, (b + 1) * BP)

        def cnt(p, b, per, i=0):
            return p * (NB * per) + (b * per + i)

        block = ctx.enter_context(nc.Block())

        @block.sync
        def _(sp):
            def load(p, half, b):
                sp.dma_start(X[:, half, :, px(b)], x_v[p, :, :, px(b)]).then_inc(loaded[b], 16)

            def store(p, half, b):
                at_least(sp, out_ok, 2 + cnt(p, b, KC, KC))
                sp.dma_start(o_v[p, :, :, px(b)], X[:, half, :, px(b)]).then_inc(stored[b], 16)

            def period(p, half, more):
                for b in range(NB):
                    store(p - 1, 1 - half, b)
                    if more:
                        at_least(sp, stored[b], 16 * p)
                        load(p + 1, 1 - half, b)

            for b in range(NB):
                load(0, 0, b)
            sp.dma_start(dict_rows, dic.rearrange("(k n) c -> n k c", n=P)).then_inc(const_in, 16)
            sp.dma_start(pw_raw, w_pwT.rearrange("(k c) n -> c k n", c=P)).then_inc(const_in, 16)
            sp.dma_start(wd[:], w_dw.rearrange("(k c) o i j -> c k (o i j)", c=P)).then_inc(const_in, 16)
            for i, v in enumerate(bn):
                sp.dma_start(bnv[:, i, :], v).then_inc(const_in, 16)
            sp.dma_start(table[1:ND + 1, :], dic).then_inc(table_in, 16)
            sp.wait_ge(zero_ok, 1)
            sp.dma_start(table[0:1, :], zero_row).then_inc(table_in, 16)
            sp.wait_ge(dve_setup, 6)
            for b in range(NB):
                load(1, 1, b)
            with sp.Fori(0, NI // 2 - 1) as pair:
                p = pair * 2 + 1
                period(p, 1, True)
                period(p + 1, 0, True)
            period(NI - 1, 1, False)
            period(NI, 0, False)
            for b in range(NB):
                sp.wait_ge(stored[b], 16 * NI)

        @block.gpsimd
        def _(pool):
            pool.memset(g_ring[:, 0, :], 0.0).then_inc(zero_ok, 1)
            pool.sem_inc(begun, 1)
            pool.memset(ident[:], 0.0).then_inc(id_ok, 1)
            pool.memset(group_mean[:], 1.0 / GROUP).then_inc(id_ok, 1)
            pool.memset(ones16[:], 1.0).then_inc(pool_setup, 1)
            pool.memset(plane[:], 0.0).then_inc(pool_setup, 1)
            pool.wait_ge(id_ok, 2)
            pool.affine_select(out=ident[:], in_=ident[:], compare_op=ALU.not_equal, fill=1.0, base=0,
                               pattern=[[-1, P]], channel_multiplier=1).then_inc(id_ok, 1)
            gv = group_mean[:].rearrange("p (a c) -> p a c", c=GROUP)
            pool.affine_select(out=gv, in_=gv, compare_op=ALU.is_ge, fill=0.0, base=0,
                               pattern=[[-GROUP, P // GROUP], [0, GROUP]],
                               channel_multiplier=1).then_inc(id_ok, 1)
            pool.wait_ge(id_ok, 4)
            pool.tensor_copy(ident16[:], ident[:]).then_inc(pool_setup, 1)
            pool.affine_select(out=gv, in_=gv, compare_op=ALU.is_ge, fill=0.0, base=GROUP - 1,
                               pattern=[[GROUP, P // GROUP], [0, GROUP]],
                               channel_multiplier=-1).then_inc(pool_setup, 1)

            def prepare(p, b):
                s = b % 2

                def add_squares(k):
                    pool.wait_ge(sq_ok, cnt(p, b, KC, k + 1))
                    at_least(pool, acc, cnt(p, b, 5, k - 1))
                    pool.tensor_tensor(sq_sum[:], sq_ring[:, 0] if k == 1 else sq_sum[:],
                                       sq_ring[:, k % 2], ALU.add).then_inc(acc, 1)

                for k in range(KC):
                    pool.wait_ge(g_ok, cnt(p, b, KC, k + 1))
                    pool.wait_ge(hi_ok, cnt(p, b, KC, k + 1))
                    pool.tensor_tensor(g_lo[:, s, k], g_ring[:, k % 2], g_hi[:, s, k],
                                       ALU.subtract).then_inc(lo_ok, 1)
                    if k == 1:
                        add_squares(1)
                add_squares(2)
                add_squares(3)
                wait_apart(pool, begun, (acc, cnt(p, b, 5, 3)))
                pool.tensor_copy(sq_hi[:, s], sq_sum[:]).then_inc(acc, 1)
                pool.wait_ge(acc, cnt(p, b, 5, 4))
                pool.tensor_tensor(sq_lo[:, s], sq_sum[:], sq_hi[:, s], ALU.subtract).then_inc(acc, 1)

            def gather(p, b):
                s = b % 2
                wait_apart(pool, begun, (pick, cnt(p, b, 4, 4)),
                                        (back_ok, cnt(p, b - 1, KC)))
                for t in range(NT):
                    pool.indirect_dma_start(rows[:, s, t, :], None, table[:, :],
                                            bass.IndirectOffsetOnAxis(row_at[:, s, t:t + 1], 0)
                                            ).then_inc(gathered[s], 16)

            def period(p):
                prepare(p, 0)
                for b in range(NB):
                    if b + 1 < NB:
                        prepare(p, b + 1)
                    gather(p, b)

            pool.wait_ge(table_in, 32)
            pool.wait_ge(pe_setup, 4)
            period(0)
            with pool.Fori(0, NI // 2 - 1) as pair:
                p = pair * 2 + 1
                period(p)
                period(p + 1)
            period(NI - 1)

        @block.scalar
        def _(act):
            a = nc.scalar
            act.wait_ge(const_in, 16 * 11)
            for k in range(KC):
                a.activation(X[:, 1, 1, px(k)], dict_rows[:, k], ACT.Square,
                             accum_out=d_n2[:, k:k + 1]).then_inc(act_setup, 1)
            a.activation(wds[:], wd[:], ACT.Sign).then_inc(act_setup, 1)
            a.activation(pw[:], pw_raw, ACT.Sign, saturate=False).then_inc(act_setup, 1)
            act.wait_ge(act_setup, KC)
            a.activation(d_r[:], d_n2[:], ACT.Sqrt).then_inc(act_roots, 1)
            act.wait_ge(dve_setup, 1)
            a.activation(bn_r[:], bn_a[:], ACT.Sqrt).then_inc(act_roots, 1)
            for k in range(KC):
                act.wait_ge(pe_setup, k + 1)
                a.activation(dT_hi[:, k], sim[k % 2][:], ACT.Copy).then_inc(act_split, 1)

            def root_of_variance(p):
                act.wait_ge(stat, p * STAT_STEPS + 4)
                a.activation(root[:], var[:], ACT.Sqrt).then_inc(stat_root, 1)

            def high(p, half, b, k):
                s = b % 2
                at_least(act, sim_ok, cnt(p, b - 1, NT))
                a.activation(g_hi[:, s, k], X[:, half, k, px(b)], ACT.Identity,
                             bias=aff_g[:, 1, k:k + 1], scale=aff_g[:, 0, k:k + 1]).then_inc(hi_ok, 1)

            def square(p, half, b, k):
                if k >= 2:
                    act.wait_ge(acc, cnt(p, b, 5, 1))
                else:
                    at_least(act, acc, cnt(p, b - 1, 5, 3))
                a.activation(sq_ring[:, k % 2], X[:, half, k, px(b)], ACT.Square,
                             bias=aff_q[:, 1, k:k + 1], scale=aff_q[:, 0, k:k + 1]).then_inc(sq_ok, 1)

            def g_again(p, half, b, k):
                at_least(act, sel_ok, cnt(p, b, KC, k - 1))
                a.activation(g_sel[:, k % 2], X[:, half, k, px(b)], ACT.Identity,
                             bias=aff[:, 1, k:k + 1], scale=aff[:, 0, k:k + 1]).then_inc(gsel_ok, 1)

            def signs(q, half, b, k):
                wait_apart(act, begun, (mean_step, 2 * q + 2 if b == 0 and k == 0 else 0))
                a.activation(plane[:, k, 1 + b * ROWS:1 + (b + 1) * ROWS, 1:1 + W],
                             X[:, half, k, px(b)].rearrange("p (h w) -> p h w", w=W),
                             ACT.Sign, bias=neg_mean[:, k:k + 1], scale=1.0,
                             saturate=False).then_inc(sign_ok, 1)

            def mids(q, b, k):
                wait_apart(act, begun, (dw_ok, cnt(q, b, KC, k + 1)),
                                       (pw_ok, cnt(q, b - 1, KC) if b >= 2 else 0))
                a.activation(mid[:, b % 2, k], dwp[k % 2][:], ACT.Sign, bias=bn_b[:, 0, k:k + 1],
                             scale=bn_i[:, 0, k:k + 1], saturate=False).then_inc(mid_ok, 1)

            def second_norm(q, b, k):
                act.wait_ge(pw_ok, cnt(q, b, KC, k + 1))
                a.activation(pwp[k % 2][:], pwp[k % 2][:], ACT.Identity, bias=bn_b[:, 1, k:k + 1],
                             scale=bn_i[:, 1, k:k + 1]).then_inc(y_ok, 1)

            def after_taps(q, i):
                mids(q, i // KC, i % KC)
                if i >= KC:
                    second_norm(q, i // KC - 1, i % KC)

            def period(p, half, match, conv):
                q, old = p - 1, 1 - half
                if conv:
                    for i in range(KC):
                        after_taps(q, i)
                        signs(q, old, 2, i)
                    for k in range(KC):
                        if match and k == 3:
                            root_of_variance(p)
                        after_taps(q, KC + k)
                        signs(q, old, 3, k)
                elif match:
                    root_of_variance(p)
                if match:
                    act.wait_ge(stat, p * STAT_STEPS + 9)
                    for k in range(KC):
                        high(p, half, 0, k)
                        square(p, half, 0, k)
                for b in range(NB):
                    ahead = match and b + 1 < NB
                    for t in range(NT):
                        if ahead and t < 2:
                            high(p, half, b + 1, 2 * t)
                            high(p, half, b + 1, 2 * t + 1)
                        if ahead and t in (0, 2):
                            square(p, half, b + 1, t)
                            square(p, half, b + 1, t + 1)
                        if match:
                            past, k = (b - 2, t + 2) if t < 2 else (b - 1, t - 2)
                            if past >= 0:
                                g_again(p, half, past, k)
                        if conv and t % 2:
                            after_taps(q, 2 * KC + 2 * b + t // 2)
                        if conv and t == 2:
                            signs(q, old, 4 + b // 2, 2 * (b % 2))
                            signs(q, old, 4 + b // 2, 2 * (b % 2) + 1)
                for i in range(2 * KC):
                    if match and i < KC:
                        g_again(p, half, NB - 2 + i // 2, (i + 2) % KC)
                    if conv:
                        after_taps(q, (NB - 2) * KC + i)
                    if match and KC <= i < KC + 2:
                        g_again(p, half, NB - 1, i - 2)
                if conv:
                    for k in range(KC):
                        second_norm(q, NB - 1, k)
                if match:
                    for k in range(KC):
                        signs(p, half, 0, k)
                        signs(p, half, 1, k)

            act.wait_ge(pool_setup, 4)
            act.wait_ge(dve_setup, 5)
            period(0, 0, True, False)
            with act.Fori(0, NI // 2 - 1) as pair:
                p = pair * 2 + 1
                period(p, 1, True, True)
                period(p + 1, 0, True, True)
            period(NI - 1, 1, True, True)
            period(NI, 0, False, True)

        @block.vector
        def _(dve):
            v = nc.vector

            dve.wait_ge(const_in, 16 * 11)
            eps_in = bnv[:, 3:8:4, :]
            v.tensor_scalar(bn_a[:], eps_in, BN_EPS, None, ALU.add).then_inc(dve_setup, 1)
            dve.wait_ge(act_roots, 1)
            own = sem("own")
            steps = [0]

            def then(ins):
                steps[0] += 1
                ins.then_inc(own, 1)
                dve.wait_ge(own, steps[0])

            then(v.reciprocal(d_q[:], d_r[:]))
            then(v.tensor_tensor(d_q[:], d_n2[:], d_q[:], ALU.mult))
            then(v.tensor_tensor(d_s[:], d_q[:], d_r[:], ALU.add))
            then(v.reciprocal(d_s[:], d_s[:]))
            for k in range(KC):
                last = v.tensor_scalar(unit_rows[:, k], dict_rows[:, k], d_s[:, k:k + 1], 2 * D_SCALE,
                                       ALU.mult, ALU.mult)
            last.then_inc(dve_setup, 1)
            dve.wait_ge(act_roots, 2)
            then(v.reciprocal(bn_q[:], bn_r[:]))
            then(v.tensor_tensor(bn_q[:], bn_a[:], bn_q[:], ALU.mult))
            then(v.tensor_tensor(bn_s[:], bn_q[:], bn_r[:], ALU.add))
            then(v.reciprocal(bn_s[:], bn_s[:]))
            then(v.scalar_tensor_tensor(bn_i[:], bnv[:, 0:5:4, :], 2.0, bn_s[:], ALU.mult, ALU.mult))
            then(v.tensor_tensor(bn_m[:], bnv[:, 2:7:4, :], bn_i[:], ALU.mult))
            v.tensor_tensor(bn_b[:], bnv[:, 1:6:4, :], bn_m[:], ALU.subtract).then_inc(dve_setup, 1)
            dve.wait_ge(pool_setup, 4)
            dve.wait_ge(act_setup, KC + 1)
            for k in range(KC):
                for tap in range(9):
                    last = v.tensor_scalar(diag[:, k, tap], ident16[:], wds[:, k, tap:tap + 1], None,
                                           ALU.mult, saturate=False)
            last.then_inc(dve_setup, 1)
            for k in range(KC):
                dve.wait_ge(act_split, k + 1)
                v.tensor_tensor(dT_lo[:, k], sim[k % 2][:], dT_hi[:, k], ALU.subtract).then_inc(dve_split, 1)
            dve.wait_ge(act_setup, KC + 2)
            v.memset(x_sums[:], 0.0).then_inc(dve_setup, 2)
            v.memset(q_min[:], 0.0).then_inc(out_ok, 2)

            def chunk_stats(p, half, b, k):
                wait_apart(dve, begun, (loaded[b], 16 * (p + 1)))
                v.bn_stats(bn6[:, k, b, :], X[:, half, k, px(b)]).then_inc(stat_bn, 1)

            def group_means(p):
                n = p * STAT_STEPS
                wait_apart(dve, begun, (stat_bn, NB * KC * (p + 1)))
                for k in range(KC):
                    ins = v.bn_aggr(mv[:, k, :], bn6[:, k, :, :])
                ins.then_inc(stat, 1)

            def group_spread(p):
                n = p * STAT_STEPS
                dve.wait_ge(stat, n + 1)
                dve.wait_ge(stat_mm, 2 * p + 1)
                v.tensor_copy(gm[:], misc[:, 0:KC])
                v.tensor_tensor(dev[:], mv[:, :, 0], misc[:, 0:KC], ALU.subtract).then_inc(stat, 1)
                dve.wait_ge(stat, n + 2)
                v.tensor_tensor(dev2[:], dev[:], dev[:], ALU.mult).then_inc(stat_own, 1)
                dve.wait_ge(stat_own, 4 * p + 1)
                v.tensor_tensor(spread[:], dev2[:], mv[:, :, 1], ALU.add).then_inc(stat, 1)

            def group_scale(p):
                n = p * STAT_STEPS
                dve.wait_ge(stat_mm, 2 * p + 2)
                v.tensor_scalar(var[:], misc[:, KC:2 * KC], GN_EPS, None, ALU.add).then_inc(stat, 1)
                dve.wait_ge(stat, n + 4)
                dve.wait_ge(stat_root, p + 1)
                v.reciprocal(quot[:], root[:]).then_inc(stat_own, 1)
                dve.wait_ge(stat_own, 4 * p + 2)
                v.tensor_tensor(quot[:], var[:], quot[:], ALU.mult).then_inc(stat, 1)
                dve.wait_ge(stat, n + 5)
                v.tensor_tensor(std[:], quot[:], root[:], ALU.add).then_inc(stat, 1)
                dve.wait_ge(stat, n + 6)
                v.reciprocal(dev[:], std[:]).then_inc(stat_own, 1)
                dve.wait_ge(stat_own, 4 * p + 3)
                v.tensor_scalar(aff[:, 0, :], dev[:], 2.0, None, ALU.mult).then_inc(stat, 1)
                dve.wait_ge(stat, n + 7)
                v.scalar_tensor_tensor(aff[:, 1, :], gm[:], -1.0, aff[:, 0, :], ALU.mult,
                                       ALU.mult).then_inc(stat_own, 1)
                dve.wait_ge(stat_own, 4 * p + 4)
                v.tensor_scalar(aff_g[:], aff[:], G_SCALE, None, ALU.mult).then_inc(stat, 1)
                v.tensor_scalar(aff_q[:], aff[:], SQ_SCALE, None, ALU.mult).then_inc(stat, 1)
                dve.wait_ge(stat, n + 9)

            def norm_chunk(p, half, b, k):
                at_least(dve, lo_ok, cnt(p, b, KC, k - 1))
                v.tensor_scalar(g_ring[:, k % 2], X[:, half, k, px(b)], gm[:, k:k + 1],
                                aff_g[:, 0, k:k + 1], ALU.subtract, ALU.mult).then_inc(g_ok, 1)

            def take_norm(p, b):
                dve.wait_ge(norm_ok, cnt(p, b, 1, 1))
                v.tensor_copy(n2[:, b % 2], misc[:, 0:NT]).then_inc(norm_used, 1)

            def top(p, b, t):
                wait_apart(dve, begun, (sim_ok, cnt(p, b, NT, t + 1)))
                v.max(tops[:, b % 2, t], sim[t % 2][:]).then_inc(top_ok, 1)

            def where(p, b, t):
                wait_apart(dve, begun, (top_ok, cnt(p, b, NT, t + 1)))
                v.max_index(top_at[:, b % 2, t], tops[:, b % 2, t], sim[t % 2][:]).then_inc(top_used, 1)

            def choose(p, b):
                s = b % 2
                m = tops[:, s, :, 0]
                dve.wait_ge(top_used, cnt(p, b, NT, NT))
                dve.wait_ge(norm_used, cnt(p, b, 1, 1))
                v.scalar_tensor_tensor(q_min[:], m, 0.0, m, ALU.min, ALU.mult).then_inc(pick, 1)
                dve.wait_ge(pick, cnt(p, b, 4, 1))
                v.scalar_tensor_tensor(taken[:], q_min[:], Q_FACTOR, n2[:, s], ALU.mult,
                                       ALU.is_lt).then_inc(pick, 1)
                dve.wait_ge(pick, cnt(p, b, 4, 2))
                v.tensor_scalar(kept[:, s], taken[:], -1.0, 1.0, ALU.mult, ALU.add).then_inc(pick, 1)
                v.scalar_tensor_tensor(row_at[:, s], top_at[:, s, :, 0], 1.0, taken[:], ALU.add,
                                       ALU.mult).then_inc(pick, 1)

            def keep(p, half, b, k):
                wait_apart(dve, begun, (kept_ok, cnt(p, b, 1, 1)),
                                       (gsel_ok, cnt(p, b, KC, k + 1)),
                                       (back_ok, cnt(p, b, KC, k + 1)))
                v.copy_predicated(back[:], misc[:].bitcast(I32), g_sel[:, k % 2]).then_inc(sel_ok, 1)

            def residual(p, half, b, k):
                dve.wait_ge(sel_ok, cnt(p, b, KC, k + 1))
                xv = X[:, half, k, px(b)]
                v.scalar_tensor_tensor(xv, back[:], 1.0, xv, ALU.mult, ALU.add,
                                       accum_out=x_sums[:, k, b:b + 1]).then_inc(x1_ok, 1)

            def finish(q, half, b, k):
                dve.wait_ge(y_ok, cnt(q, b, KC, k + 1))
                xv = X[:, half, k, px(b)]
                v.tensor_tensor(xv, pwp[k % 2][:], xv, ALU.add).then_inc(out_ok, 1)

            def period(p, half, match, conv, stats):
                q, old = p - 1, 1 - half
                if match and conv:
                    for b in (NB - 2, NB - 1):
                        for k in range(KC):
                            chunk_stats(p, half, b, k)
                if match:
                    group_means(p)
                if conv:
                    finish(q, old, 0, 0)
                if match:
                    group_spread(p)
                if conv:
                    finish(q, old, 0, 1)
                    finish(q, old, 0, 2)
                if match:
                    group_scale(p)
                    norm_chunk(p, half, 0, 0)
                    norm_chunk(p, half, 0, 1)
                if conv:
                    finish(q, old, 0, 3)
                if match:
                    norm_chunk(p, half, 0, 2)
                    norm_chunk(p, half, 0, 3)
                for b in range(NB):
                    for t in range(NT):
                        ahead = match and b + 1 < NB and t < 2
                        past, k = (b - 2, t + 1) if t < 3 else (b - 1, 0)
                        if match:
                            top(p, b, t)
                        if ahead:
                            norm_chunk(p, half, b + 1, 2 * t)
                        if match:
                            where(p, b, t)
                        if match and t == 3:
                            take_norm(p, b)
                            choose(p, b)
                        if ahead:
                            norm_chunk(p, half, b + 1, 2 * t + 1)
                        if match and past >= 0:
                            keep(p, half, past, k)
                        if conv and t % 2:
                            i = KC + 2 * b + t // 2
                            finish(q, old, i // KC, i % KC)
                        if stats and t % 2 == 0 and b:
                            i = 2 * (b - 1) + t // 2
                            chunk_stats(p + 1, old, i // KC, i % KC)
                        if match and past >= 0:
                            residual(p, half, past, k)
                for i in range(2 * KC):
                    past, k = (NB - 2, i + 1) if i < KC - 1 else (NB - 1, i - KC)
                    if match and i != KC - 1:
                        keep(p, half, past, k)
                    if conv:
                        finish(q, old, NB - 3 + i // KC, i % KC)
                    if match and i != KC - 1:
                        residual(p, half, past, k)
                    if stats and i < 6:
                        n = 3 * KC + 2 + i
                        chunk_stats(p + 1, old, n // KC, n % KC)
                if match:
                    dve.wait_ge(x1_ok, cnt(p, NB, KC))
                    at_least(dve, sign_ok, NB * KC * p)
                    v.reduce_sum(x_sum[:], x_sums[:], AX.X).then_inc(mean_step, 1)
                if conv:
                    for k in range(KC - 1):
                        finish(q, old, NB - 1, k)
                if match:
                    dve.wait_ge(mean_mm, p + 1)
                    v.tensor_scalar(neg_mean[:], misc[:, 0:KC], -1.0 / PIX, None,
                                    ALU.mult).then_inc(mean_step, 1)
                if conv:
                    finish(q, old, NB - 1, KC - 1)
                if stats:
                    for k in range(KC):
                        chunk_stats(p + 1, old, NB - 3, k)

            stat_own = sem("stat_own")
            dve.wait_ge(table_in, 32)
            for b in range(NB):
                for k in range(KC):
                    chunk_stats(0, 0, b, k)
            period(0, 0, True, False, True)
            with dve.Fori(0, NI // 2 - 1) as pair:
                p = pair * 2 + 1
                period(p, 1, True, True, True)
                period(p + 1, 0, True, True, True)
            period(NI - 1, 1, True, True, False)
            period(NI, 0, False, True, False)

        @block.tensor
        def _(pe):
            t_ = nc.tensor
            pe.wait_ge(pool_setup, 4)
            pe.wait_ge(dve_setup, 2)
            for k in range(KC):
                if k >= 2:
                    pe.wait_ge(dve_split, k - 1)
                for n in range(KC):
                    last = t_.transpose(sim[k % 2][:, n * P:(n + 1) * P],
                                        unit_rows[:, n, k * P:(k + 1) * P], ident[:])
                last.then_inc(pe_setup, 1)
            pe.wait_ge(dve_split, KC)
            pe.wait_ge(dve_setup, 6)

            def means(p):
                pe.wait_ge(stat, p * STAT_STEPS + 1)
                t_.matmul(misc[:, 0:KC], group_mean[:], mv[:, :, 0], start=True,
                          stop=True).then_inc(stat_mm, 1)

            def spreads(p):
                pe.wait_ge(stat, p * STAT_STEPS + 3)
                t_.matmul(misc[:, KC:2 * KC], group_mean[:], spread[:], start=True,
                          stop=True).then_inc(stat_mm, 1)

            def norms(p, b):
                s = b % 2
                pe.wait_ge(acc, cnt(p, b, 5, 5))
                at_least(pe, sel_ok, cnt(p, b - 1, KC))
                if b == 0:
                    pe.wait_ge(stat, p * STAT_STEPS + 4)
                for t in range(NT):
                    px_t = slice(t * P, (t + 1) * P)
                    t_.matmul(misc[:, t:t + 1], sq_hi[:, s, px_t], ones16[:], start=True, stop=False)
                    last = t_.matmul(misc[:, t:t + 1], sq_lo[:, s, px_t], ones16[:], start=False,
                                     stop=True)
                last.then_inc(norm_ok, 1)

            def products(p, b, t):
                s = b % 2
                if t == 0:
                    pe.wait_ge(hi_ok, cnt(p, b, KC, KC))
                    pe.wait_ge(lo_ok, cnt(p, b, KC, KC))
                at_least(pe, top_used, cnt(p, b, NT, t - 1))
                px_t = slice(t * P, (t + 1) * P)
                for k in range(KC):
                    t_.matmul(sim[t % 2][:], g_hi[:, s, k, px_t], dT_hi[:, k], start=(k == 0), stop=False)
                    t_.matmul(sim[t % 2][:], g_hi[:, s, k, px_t], dT_lo[:, k], start=False, stop=False)
                    last = t_.matmul(sim[t % 2][:], g_lo[:, s, k, px_t], dT_hi[:, k], start=False,
                                     stop=(k == KC - 1))
                last.then_inc(sim_ok, 1)

            def spread_kept(p, b):
                s = b % 2
                pe.wait_ge(pick, cnt(p, b, 4, 3))
                at_least(pe, sel_ok, cnt(p, b, KC))
                pe.wait_ge(norm_used, cnt(p, min(b + 1, NB - 1), 1, 1))
                for t in range(NT):
                    last = t_.matmul(misc[:, t * P:(t + 1) * P],
                                     kept[:, s, t:t + 1].to_broadcast([P, P]), ident16[:],
                                     start=True, stop=True)
                last.then_inc(kept_ok, 1)

            def transpose_back(p, b, k):
                s = b % 2
                if k == 0:
                    spread_kept(p, b)
                    pe.wait_ge(gathered[s], p * (16 * NT * NB // 2) + 16 * NT * (b // 2 + 1))
                at_least(pe, x1_ok, cnt(p, b, KC, k))
                for t in range(NT):
                    last = t_.transpose(back[:, t * P:(t + 1) * P], rows[:, s, t, k * P:(k + 1) * P],
                                        ident[:])
                last.then_inc(back_ok, 1)

            def stream_mean(p):
                pe.wait_ge(mean_step, 2 * p + 1)
                t_.matmul(misc[:, 0:KC], group_mean[:], x_sum[:], start=True,
                          stop=True).then_inc(mean_mm, 1)

            def depthwise(q, b, k):
                needed = 2 * (k + 1) if b == 0 else min((b + 1) * KC + k + 1, NB * KC)
                wait_apart(pe, begun, (sign_ok, q * NB * KC + needed),
                                      (mid_ok, cnt(q, b, KC, k - 1) if b or k >= 2 else 0))
                for tap in range(9):
                    dy, dx = tap // 3, tap % 3
                    last = t_.matmul(dwp[k % 2][:], diag[:, k, tap],
                                     plane[:, k, b * ROWS + dy:b * ROWS + dy + ROWS, dx:dx + W],
                                     start=(tap == 0), stop=(tap == 8))
                last.then_inc(dw_ok, 1)

            def pointwise(q, b, n):
                wait_apart(pe, begun, (mid_ok, cnt(q, b, KC, KC) if n == 0 else 0),
                                      (out_ok, cnt(q, b, KC, n + 1)))
                for k in range(KC):
                    last = t_.matmul(pwp[n % 2][:], pw[:, k, n * P:(n + 1) * P], mid[:, b % 2, k],
                                     start=(k == 0), stop=(k == KC - 1))
                last.then_inc(pw_ok, 1)

            def taps(q, i):
                depthwise(q, i // KC, i % KC)
                if i >= KC:
                    pointwise(q, i // KC - 1, i % KC)

            def period(p, match, conv):
                q = p - 1
                for i in range(2 * KC):
                    if conv:
                        taps(q, i)
                    if match and i == KC:
                        means(p)
                    if match and i == KC + 1:
                        spreads(p)
                for b in range(NB):
                    for t in range(NT):
                        past, k = (b - 2, t + 1) if t < 3 else (b - 1, 0)
                        if match:
                            products(p, b, t)
                        if match and t == 3:
                            norms(p, b)
                        if conv and t % 2:
                            taps(q, 2 * KC + 2 * b + t // 2)
                        if match and past >= 0:
                            transpose_back(p, past, k)
                for i in range(2 * KC):
                    if conv:
                        taps(q, (NB - 2) * KC + i)
                    if match and i != KC - 1:
                        if i < KC:
                            transpose_back(p, NB - 2, i + 1)
                        else:
                            transpose_back(p, NB - 1, i - KC)
                if conv:
                    for n in range(KC - 1):
                        pointwise(q, NB - 1, n)
                if match:
                    stream_mean(p)
                if conv:
                    pointwise(q, NB - 1, KC - 1)

            period(0, True, False)
            with pe.Fori(0, NI // 2 - 1) as pair:
                p = pair * 2 + 1
                period(p, True, True)
                period(p + 1, True, True)
            period(NI - 1, True, True)
            period(NI, False, True)


def kernel(**inputs):
    import numpy as _np
    import concourse.bacc as _bacc
    from concourse import mybir as _mybir
    from concourse.bass_utils import run_bass_kernel_spmd as _run

    nc = _bacc.Bacc("TRN2", target_bir_lowering=False, num_devices=1, dynamic_dma_scratch_size=4096)
    arrays, args = {}, {}
    for name, value in inputs.items():
        a = _np.asarray(value)
        if name == "L1_conv_w_pw":
            a = a.reshape(C, C).transpose(1, 0)
        elif a.shape == (C,):
            a = a.reshape(KC, P).transpose(1, 0)
        a = _np.ascontiguousarray(a)
        arrays[f"in_{name}"] = a
        args[name] = nc.dram_tensor(f"in_{name}", a.shape, _mybir.dt.from_np(a.dtype),
                                    kind="ExternalInput").ap()
    out = nc.dram_tensor("out_0", (NI, C, H, W), FP32, kind="ExternalOutput").ap()
    bn = [args[f"L1_conv_{v}{i}"] for i in (1, 2) for v in "gbmv"]
    conv_net(nc, args["x"], args["L0_conv_negative_dict"], args["L1_conv_w_dw"], args["L1_conv_w_pw"],
             bn, out)
    r = _run(nc, [arrays], core_ids=[0])
    return r.results[0]["out_0"]
```
